# Optimizing a Trainium2 kernel written in Bass

```python
import numpy as np
import jax
import jax.numpy as jnp

def _softmax(x, axis=-1):
    return jax.nn.softmax(x, axis=axis)

def _gelu(x):
    return jax.nn.gelu(x, approximate=True)

def _silu(x):
    return jax.nn.silu(x)

def _sigmoid(x):
    return jax.nn.sigmoid(x)

def _layernorm(x, axis=-1, eps=1e-05):
    m = jnp.mean(x, axis=axis, keepdims=True)
    v = jnp.var(x, axis=axis, keepdims=True)
    return (x - m) / jnp.sqrt(v + eps)

def _scatter_add(tgt, idx, src, axis=0):
    return tgt.at[idx].add(src)

def _segment_sum(src, seg, n):
    return jax.ops.segment_sum(src, seg, n)
kernel_name = 'mk_dlrm_tower_d1_rec_r8_09b791'

def setup_inputs(seed: int=0):
    np.random.seed(seed)
    _w = jnp.asarray

    def _rec_inputs():
        import jax
        import jax.numpy as jnp
        _tk = jax.random.key(seed)
        dense_ctx = jax.random.normal(jax.random.fold_in(_tk, 190), (512, 16), jnp.float32)
        ids = jnp.stack([jax.random.randint(jax.random.fold_in(_tk, 200 + f), (512,), 0, v, jnp.int32) for f, v in enumerate([1250, 1000, 125000, 1000, 1000, 12500, 1250, 1000, 12500, 1250, 1250, 1250, 12500, 1000, 12500, 125000, 12500, 125000, 1250, 1000, 1250, 1000, 1000, 1000, 1000, 12500, 1250, 1000, 1000, 12500, 1250, 12500])], axis=1)
        tbl_0 = 0.05 * jax.random.normal(jax.random.fold_in(_tk, 500 + 0), (1250, 64), jnp.float32)
        tbl_1 = 0.05 * jax.random.normal(jax.random.fold_in(_tk, 500 + 1), (1000, 64), jnp.float32)
        tbl_2 = 0.05 * jax.random.normal(jax.random.fold_in(_tk, 500 + 2), (125000, 64), jnp.float32)
        tbl_3 = 0.05 * jax.random.normal(jax.random.fold_in(_tk, 500 + 3), (1000, 64), jnp.float32)
        tbl_4 = 0.05 * jax.random.normal(jax.random.fold_in(_tk, 500 + 4), (1000, 64), jnp.float32)
        tbl_5 = 0.05 * jax.random.normal(jax.random.fold_in(_tk, 500 + 5), (12500, 64), jnp.float32)
        tbl_6 = 0.05 * jax.random.normal(jax.random.fold_in(_tk, 500 + 6), (1250, 64), jnp.float32)
        tbl_7 = 0.05 * jax.random.normal(jax.random.fold_in(_tk, 500 + 7), (1000, 64), jnp.float32)
        tbl_8 = 0.05 * jax.random.normal(jax.random.fold_in(_tk, 500 + 8), (12500, 64), jnp.float32)
        tbl_9 = 0.05 * jax.random.normal(jax.random.fold_in(_tk, 500 + 9), (1250, 64), jnp.float32)
        tbl_10 = 0.05 * jax.random.normal(jax.random.fold_in(_tk, 500 + 10), (1250, 64), jnp.float32)
        tbl_11 = 0.05 * jax.random.normal(jax.random.fold_in(_tk, 500 + 11), (1250, 64), jnp.float32)
        tbl_12 = 0.05 * jax.random.normal(jax.random.fold_in(_tk, 500 + 12), (12500, 64), jnp.float32)
        tbl_13 = 0.05 * jax.random.normal(jax.random.fold_in(_tk, 500 + 13), (1000, 64), jnp.float32)
        tbl_14 = 0.05 * jax.random.normal(jax.random.fold_in(_tk, 500 + 14), (12500, 64), jnp.float32)
        tbl_15 = 0.05 * jax.random.normal(jax.random.fold_in(_tk, 500 + 15), (125000, 64), jnp.float32)
        tbl_16 = 0.05 * jax.random.normal(jax.random.fold_in(_tk, 500 + 16), (12500, 64), jnp.float32)
        tbl_17 = 0.05 * jax.random.normal(jax.random.fold_in(_tk, 500 + 17), (125000, 64), jnp.float32)
        tbl_18 = 0.05 * jax.random.normal(jax.random.fold_in(_tk, 500 + 18), (1250, 64), jnp.float32)
        tbl_19 = 0.05 * jax.random.normal(jax.random.fold_in(_tk, 500 + 19), (1000, 64), jnp.float32)
        tbl_20 = 0.05 * jax.random.normal(jax.random.fold_in(_tk, 500 + 20), (1250, 64), jnp.float32)
        tbl_21 = 0.05 * jax.random.normal(jax.random.fold_in(_tk, 500 + 21), (1000, 64), jnp.float32)
        tbl_22 = 0.05 * jax.random.normal(jax.random.fold_in(_tk, 500 + 22), (1000, 64), jnp.float32)
        tbl_23 = 0.05 * jax.random.normal(jax.random.fold_in(_tk, 500 + 23), (1000, 64), jnp.float32)
        tbl_24 = 0.05 * jax.random.normal(jax.random.fold_in(_tk, 500 + 24), (1000, 64), jnp.float32)
        tbl_25 = 0.05 * jax.random.normal(jax.random.fold_in(_tk, 500 + 25), (12500, 64), jnp.float32)
        tbl_26 = 0.05 * jax.random.normal(jax.random.fold_in(_tk, 500 + 26), (1250, 64), jnp.float32)
        tbl_27 = 0.05 * jax.random.normal(jax.random.fold_in(_tk, 500 + 27), (1000, 64), jnp.float32)
        tbl_28 = 0.05 * jax.random.normal(jax.random.fold_in(_tk, 500 + 28), (1000, 64), jnp.float32)
        tbl_29 = 0.05 * jax.random.normal(jax.random.fold_in(_tk, 500 + 29), (12500, 64), jnp.float32)
        tbl_30 = 0.05 * jax.random.normal(jax.random.fold_in(_tk, 500 + 30), (1250, 64), jnp.float32)
        tbl_31 = 0.05 * jax.random.normal(jax.random.fold_in(_tk, 500 + 31), (12500, 64), jnp.float32)
        _rk = jax.random.fold_in(_tk, 7)
        W_top1 = 0.0441942 * jax.random.normal(jax.random.fold_in(_tk, 801), (512, 512), jnp.float32)
        W_top2 = 0.0441942 * jax.random.normal(jax.random.fold_in(_tk, 802), (512, 256), jnp.float32)
        W_top3 = 0.0625 * jax.random.normal(jax.random.fold_in(_tk, 803), (256, 1), jnp.float32)
        b_top1 = jnp.zeros((512,), jnp.float32)
        b_top2 = jnp.zeros((256,), jnp.float32)
        return (dense_ctx, ids, tbl_0, tbl_1, tbl_2, tbl_3, tbl_4, tbl_5, tbl_6, tbl_7, tbl_8, tbl_9, tbl_10, tbl_11, tbl_12, tbl_13, tbl_14, tbl_15, tbl_16, tbl_17, tbl_18, tbl_19, tbl_20, tbl_21, tbl_22, tbl_23, tbl_24, tbl_25, tbl_26, tbl_27, tbl_28, tbl_29, tbl_30, tbl_31, W_top1, b_top1, W_top2, b_top2, W_top3)
    dense_ctx, ids, tbl_0, tbl_1, tbl_2, tbl_3, tbl_4, tbl_5, tbl_6, tbl_7, tbl_8, tbl_9, tbl_10, tbl_11, tbl_12, tbl_13, tbl_14, tbl_15, tbl_16, tbl_17, tbl_18, tbl_19, tbl_20, tbl_21, tbl_22, tbl_23, tbl_24, tbl_25, tbl_26, tbl_27, tbl_28, tbl_29, tbl_30, tbl_31, W_top1, b_top1, W_top2, b_top2, W_top3 = _rec_inputs()

    def _L0_rec_setup():
        import jax, jax.numpy as jnp
        import numpy as np
        BATCH = 256
        NUM_FIELDS = 32
        EMBED = 64
        NPAIRS = NUM_FIELDS * (NUM_FIELDS - 1) // 2
        ROW, COL = np.triu_indices(NUM_FIELDS, k=1)
        ROW = jnp.asarray(ROW)
        COL = jnp.asarray(COL)
        key = jax.random.key(seed)
        k1, k2 = jax.random.split(key)
        emb_inputs = jax.random.normal(k1, (BATCH, NUM_FIELDS, EMBED), dtype=jnp.float32)
        fan_in = NPAIRS * EMBED
        fan_out = EMBED * EMBED
        std = float(np.sqrt(2.0 / (fan_in + fan_out)))
        kernel = jax.random.normal(k2, (EMBED, NPAIRS, EMBED), dtype=jnp.float32) * std
        return {'emb_inputs': emb_inputs, 'kernel': kernel}
    _L0_rec_all = _L0_rec_setup()
    _L0_rec_in = {k: v for k, v in _L0_rec_all.items() if k in ('kernel',)}
    del _L0_rec_all
    return {'dense_ctx': dense_ctx, 'ids': ids, 'tbl_0': tbl_0, 'tbl_1': tbl_1, 'tbl_2': tbl_2, 'tbl_3': tbl_3, 'tbl_4': tbl_4, 'tbl_5': tbl_5, 'tbl_6': tbl_6, 'tbl_7': tbl_7, 'tbl_8': tbl_8, 'tbl_9': tbl_9, 'tbl_10': tbl_10, 'tbl_11': tbl_11, 'tbl_12': tbl_12, 'tbl_13': tbl_13, 'tbl_14': tbl_14, 'tbl_15': tbl_15, 'tbl_16': tbl_16, 'tbl_17': tbl_17, 'tbl_18': tbl_18, 'tbl_19': tbl_19, 'tbl_20': tbl_20, 'tbl_21': tbl_21, 'tbl_22': tbl_22, 'tbl_23': tbl_23, 'tbl_24': tbl_24, 'tbl_25': tbl_25, 'tbl_26': tbl_26, 'tbl_27': tbl_27, 'tbl_28': tbl_28, 'tbl_29': tbl_29, 'tbl_30': tbl_30, 'tbl_31': tbl_31, 'W_top1': W_top1, 'b_top1': b_top1, 'W_top2': W_top2, 'b_top2': b_top2, 'W_top3': W_top3, 'L0_rec_kernel': _L0_rec_in['kernel']}

def reference(dense_ctx, ids, tbl_0, tbl_1, tbl_2, tbl_3, tbl_4, tbl_5, tbl_6, tbl_7, tbl_8, tbl_9, tbl_10, tbl_11, tbl_12, tbl_13, tbl_14, tbl_15, tbl_16, tbl_17, tbl_18, tbl_19, tbl_20, tbl_21, tbl_22, tbl_23, tbl_24, tbl_25, tbl_26, tbl_27, tbl_28, tbl_29, tbl_30, tbl_31, W_top1, b_top1, W_top2, b_top2, W_top3, L0_rec_kernel):
    import jax
    import jax.numpy as jnp

    def _L0_rec_ref(emb_inputs, kernel):
        import jax, jax.numpy as jnp
        import numpy as np
        BATCH = 256
        NUM_FIELDS = 32
        EMBED = 64
        NPAIRS = NUM_FIELDS * (NUM_FIELDS - 1) // 2
        ROW, COL = np.triu_indices(NUM_FIELDS, k=1)
        ROW = jnp.asarray(ROW)
        COL = jnp.asarray(COL)
        p = emb_inputs[:, ROW]
        q = emb_inputs[:, COL]
        kp = jnp.einsum('bpj,ipj->bpi', p, kernel)
        outputs = jnp.sum(kp * q, axis=-1)
        return outputs[:, None, :]
    e = jnp.stack([tbl_0[ids[:, 0]], tbl_1[ids[:, 1]], tbl_2[ids[:, 2]], tbl_3[ids[:, 3]], tbl_4[ids[:, 4]], tbl_5[ids[:, 5]], tbl_6[ids[:, 6]], tbl_7[ids[:, 7]], tbl_8[ids[:, 8]], tbl_9[ids[:, 9]], tbl_10[ids[:, 10]], tbl_11[ids[:, 11]], tbl_12[ids[:, 12]], tbl_13[ids[:, 13]], tbl_14[ids[:, 14]], tbl_15[ids[:, 15]], tbl_16[ids[:, 16]], tbl_17[ids[:, 17]], tbl_18[ids[:, 18]], tbl_19[ids[:, 19]], tbl_20[ids[:, 20]], tbl_21[ids[:, 21]], tbl_22[ids[:, 22]], tbl_23[ids[:, 23]], tbl_24[ids[:, 24]], tbl_25[ids[:, 25]], tbl_26[ids[:, 26]], tbl_27[ids[:, 27]], tbl_28[ids[:, 28]], tbl_29[ids[:, 29]], tbl_30[ids[:, 30]], tbl_31[ids[:, 31]]], axis=1)
    z = _L0_rec_ref(e, L0_rec_kernel)
    z = z.reshape(z.shape[0], -1)
    h = jnp.concatenate([z, dense_ctx], axis=1)
    h = jnp.maximum(h @ W_top1 + b_top1, 0.0)
    h = jnp.maximum(h @ W_top2 + b_top2, 0.0)
    y = h @ W_top3
    return y

_drawn_inputs = setup_inputs


def setup_inputs(seed=0):
    import zlib

    import numpy as np

    out = dict(_drawn_inputs(seed))
    spreads = {'b_top1': (0.0, 0.1), 'b_top2': (0.0, 0.1)}
    factors = {'tbl_0': 8.0,
     'tbl_1': 8.0,
     'tbl_2': 8.0,
     'tbl_3': 8.0,
     'tbl_4': 8.0,
     'tbl_5': 8.0,
     'tbl_6': 8.0,
     'tbl_7': 8.0,
     'tbl_8': 8.0,
     'tbl_9': 8.0,
     'tbl_10': 8.0,
     'tbl_11': 8.0,
     'tbl_12': 8.0,
     'tbl_13': 8.0,
     'tbl_14': 8.0,
     'tbl_15': 8.0,
     'tbl_16': 8.0,
     'tbl_17': 8.0,
     'tbl_18': 8.0,
     'tbl_19': 8.0,
     'tbl_20': 8.0,
     'tbl_21': 8.0,
     'tbl_22': 8.0,
     'tbl_23': 8.0,
     'tbl_24': 8.0,
     'tbl_25': 8.0,
     'tbl_26': 8.0,
     'tbl_27': 8.0,
     'tbl_28': 8.0,
     'tbl_29': 8.0,
     'tbl_30': 8.0,
     'tbl_31': 8.0,
     'L0_rec_kernel': 8.0}
    for name, (base, spread) in spreads.items():
        noise = np.random.default_rng([zlib.crc32(name.encode()), seed]).standard_normal(out[name].shape)
        drawn = base * np.exp(spread * noise) if base else spread * noise
        out[name] = jnp.asarray(drawn.astype(out[name].dtype))
    for name, factor in factors.items():
        out[name] = (out[name] * factor).astype(out[name].dtype)
    return out
```

```python
from contextlib import ExitStack

import concourse.bass as bass
from concourse import mybir

F32 = mybir.dt.float32
F32R = mybir.dt.float32r
I32 = mybir.dt.int32
ALU = mybir.AluOpType
ACT = mybir.ActivationFunctionType

P = 128
FIELDS = 32
D = 64
B = 512
BT = B // P
DENSE = 16
STAGES = FIELDS // 2
PAIRS = FIELDS * (FIELDS - 1) // 2
H1, H2 = 512, 256
KC1, KC2, NC1, NC2 = 4, H1 // P, H1 // P, H2 // P

CHUNK = 16
CHUNKS = PAIRS // CHUNK
CHUNK_COLS = CHUNK * D
BLOCKS_PER_CHUNK = CHUNK // 4
RAW_BUFS = 3
SPLIT_BUFS = 20
GATHER_BUFS = 4
PSUM_BUFS = 3
PROD_BUFS = 3
LAG = 2

TILES_PER_CHUNK = 64


def pair_index(r, c):
    return r * (FIELDS - 1) - r * (r - 1) // 2 + c - r - 1


def pair_order():
    pairs = [pair_index(2 * l, 2 * l + 1) for l in range(STAGES)]
    for l in range(STAGES):
        for k in range(l):
            for c in (2 * l, 2 * l + 1):
                pairs += [pair_index(2 * k, c), pair_index(2 * k + 1, c)]
    return pairs


def z_row(t, h):
    return P * (t // TILES_PER_CHUNK) + 32 * (t % 4) + 16 * h + (t % TILES_PER_CHUNK) // 4


def steps():
    order = [("fields", 0), ("diagonal", 0)]
    for l in range(1, STAGES):
        before = min(2, l - 1) + 1
        order.insert(len(order) - (before if l > 1 else 0), ("fields", l))
        order += [("block", l, k) for k in range(l)] + [("diagonal", l)]
    return order


def tiles_of(step):
    return {"fields": 0, "block": 2, "diagonal": 1}[step[0]]


def z_layout():
    rows, spare, t = [0] * (PAIRS + DENSE), [], 0
    for step in steps():
        if step[0] == "block":
            _, l, k = step
            for c in (2 * l, 2 * l + 1):
                for h in (0, 1):
                    rows[z_row(t, h)] = pair_index(2 * k + h, c)
                t += 1
        elif step[0] == "diagonal":
            l = step[1]
            rows[z_row(t, 0)] = pair_index(2 * l, 2 * l + 1)
            rows[z_row(t, 1)] = PAIRS + l
            spare.append((l, z_row(t, 1)))
            t += 1
    return rows, spare


def split_schedule():
    order = steps()
    before = {0: [0, 1]}
    n, per_stage = 2, [4, 4, 4, 3, 3, 2, 2, 2, 2, 3]
    for l, count in enumerate(per_stage):
        at = order.index(("diagonal", l)) + 1
        before.setdefault(at, []).extend(range(n, n + count))
        n += count
    assert n == CHUNKS
    return before


def build(nc, dense_t, ids, tables, k_pairs, w1, w2, b1_b2_w3, out):
    order = steps()
    split_before = split_schedule()
    _, spare_rows = z_layout()
    products = [i for i, s in enumerate(order) if s[0] != "fields"]
    product_no = {i: n for n, i in enumerate(products)}
    first_tile = {}
    t = 0
    for i, s in enumerate(order):
        first_tile[i] = t
        t += tiles_of(s)
    stage_products = [sum(1 for s in order if s[0] != "fields" and s[1] <= l) for l in range(STAGES)]
    block_product = {(s[1], s[2]): product_no[i] for i, s in enumerate(order) if s[0] == "block"}
    blocks = [(l, k) for l in range(STAGES) for k in range(l)]

    def z_chunks_ended(i):
        a, b = first_tile[i], first_tile[i] + tiles_of(order[i])
        return list(range(a // TILES_PER_CHUNK, b // TILES_PER_CHUNK))

    with ExitStack() as ctx:
        def sb(name, shape, dt=F32):
            return ctx.enter_context(nc.sbuf_tensor(name, shape, dt))

        def sem(name):
            return ctx.enter_context(nc.semaphore(name))

        ids_sb = sb("ids_sb", [P, BT, FIELDS], I32)
        gathered = sb("gathered", [P, GATHER_BUFS, 2, BT, D])
        k_raw = sb("k_raw", [P, RAW_BUFS, CHUNK_COLS])
        k_split = sb("k_split", [P, SPLIT_BUFS, CHUNK_COLS], F32R)
        k_diag = sb("k_diag", [P, CHUNK_COLS + D], F32R)
        twice = sb("twice", [P, 2, 2, BT, 2, D])
        e_hi = sb("e_hi", [P, 2, 2, B], F32R)
        e_lo = sb("e_lo", [P, 2, 2, B], F32R)
        e_pair = sb("e_pair", [P, STAGES, B])
        prod = sb("prod", [P, PROD_BUFS, 2 * B])
        select = sb("select", [P, 16, 32])
        ident = sb("ident", [P, P])
        z_sb = sb("z_sb", [P, KC1, B])
        w1_sb = sb("w1_sb", [P, KC1, H1])
        w2_sb = sb("w2_sb", [P, KC2, H2])
        columns = sb("columns", [P, NC1 + 2 * NC2])
        b1_sb = columns[:, 0:NC1]
        b2_sb = columns[:, NC1:NC1 + NC2]
        w3_sb = columns[:, NC1 + NC2:]
        h1_sb = e_pair[:, 0:NC1, :]
        h2_sb = e_pair[:, NC1:NC1 + NC2, :]
        y_sb = e_pair[0:1, NC1 + NC2, :]

        slots = [ctx.enter_context(nc.psum_tensor(f"slot{i}", [P, 2 * B], F32)) for i in range(PSUM_BUFS)]
        z_ps = [ctx.enter_context(nc.psum_tensor(f"z_ps{i}", [P, B], F32)) for i in range(2)]

        ids_in = sem("ids_in")
        k_in = [sem(f"k_in{i}") for i in range(RAW_BUFS)]
        gather_in = [sem(f"gather_in{i}") for i in range(GATHER_BUFS)]
        weights_in = sem("weights_in")
        dense_in = [sem(f"dense_in{kc}") for kc in range(KC1)]
        y_out = sem("y_out")
        zeros_made = sem("zeros_made")
        consts_made = sem("consts_made")
        select_made = sem("select_made")
        k_hi_made = sem("k_hi_made")
        k_lo_made = sem("k_lo_made")
        rows_doubled = sem("rows_doubled")
        fields_turned = sem("fields_turned")
        e_hi_made = sem("e_hi_made")
        e_lo_made = sem("e_lo_made")
        e_pair_made = sem("e_pair_made")
        forms_made = sem("forms_made")
        products_made = sem("products_made")
        products_summed = sem("products_summed")
        z_copied = sem("z_copied")
        h1_summed = sem("h1_summed")
        h1_made = sem("h1_made")
        h2_summed = sem("h2_summed")
        h2_made = sem("h2_made")
        y_summed = sem("y_summed")
        y_copied = sem("y_copied")

        def split_place(n):
            return k_split[:, (n - 1) % SPLIT_BUFS, :] if n else k_diag[:, 0:CHUNK_COLS]

        def free_slot(eng, i):
            if i < PSUM_BUFS:
                return
            old = order[i - PSUM_BUFS]
            if old[0] == "fields":
                eng.wait_ge(e_pair_made, old[1] + 1)
                eng.wait_ge(e_lo_made, old[1] + 1)
            else:
                eng.wait_ge(products_made, product_no[i - PSUM_BUFS] + 1)

        def free_split_place(eng, n):
            if n > SPLIT_BUFS:
                l, k = blocks[(n - SPLIT_BUFS) * BLOCKS_PER_CHUNK - 1]
                eng.wait_ge(forms_made, block_product[(l, k)] + 1)

        def free_e(eng, l):
            if l >= 2:
                eng.wait_ge(forms_made, stage_products[l - 2])

        def h_ps(n):
            return slots[(len(order) + n // 2) % PSUM_BUFS][:, (n % 2) * B:(n % 2 + 1) * B]

        block = ctx.enter_context(nc.Block())

        @block.sync
        def _(sp):
            sp.dma_start(ids_sb[:], ids.rearrange("(t p) f -> p t f", p=P)).then_inc(ids_in, 16)
            for n in range(CHUNKS):
                if n >= RAW_BUFS:
                    sp.wait_ge(k_lo_made, n - RAW_BUFS + 1)
                src = k_pairs[:, n * CHUNK:(n + 1) * CHUNK, :].rearrange("i p j -> i (p j)")
                for h in (0, 1):
                    sp.dma_start(k_raw[h * D:(h + 1) * D, n % RAW_BUFS, :], src).then_inc(k_in[n % RAW_BUFS], 16)
            sp.dma_start(w1_sb[:], w1.rearrange("(c p) n -> p c n", p=P)).then_inc(weights_in, 16)
            sp.dma_start(w2_sb[:], w2.rearrange("(c p) n -> p c n", p=P)).then_inc(weights_in, 16)
            sp.dma_start(columns[:], b1_b2_w3).then_inc(weights_in, 16)
            for kc in range(KC1):
                sp.wait_ge(z_copied, kc + 1)
                for l, row in spare_rows:
                    if row // P == kc:
                        sp.dma_start(z_sb[row % P:row % P + 1, kc, :], dense_t[l:l + 1, :]).then_inc(dense_in[kc], 16)
            sp.wait_ge(y_copied, 1)
            sp.dma_start(out.rearrange("b o -> o b"), y_sb).then_inc(y_out, 16)
            sp.wait_ge(y_out, 16)

        @block.gpsimd
        def _(pool):
            nc.gpsimd.memset(ident[:], 0.0).then_inc(zeros_made, 1)
            pool.wait_ge(zeros_made, 1)
            nc.gpsimd.affine_select(out=ident[:], in_=ident[:], compare_op=ALU.not_equal, fill=1.0, base=0,
                                    pattern=[[-1, P]], channel_multiplier=1).then_inc(consts_made, 1)
            pool.wait_ge(ids_in, 16)
            for l in range(STAGES):
                if l >= GATHER_BUFS:
                    pool.wait_ge(rows_doubled, l - GATHER_BUFS + 1)
                for f in (0, 1):
                    for t in range(BT):
                        field = 2 * l + f
                        nc.gpsimd.indirect_dma_start(
                            gathered[:, l % GATHER_BUFS, f, t, :], None, tables[field],
                            bass.IndirectOffsetOnAxis(ap=ids_sb[:, t, field:field + 1], axis=0),
                        ).then_inc(gather_in[l % GATHER_BUFS], 16)

        @block.scalar
        def _(act):
            def k_hi(n):
                act.wait_ge(k_in[n % RAW_BUFS], 32 * (n // RAW_BUFS + 1))
                free_split_place(act, n)
                nc.scalar.copy(split_place(n), k_raw[:, n % RAW_BUFS, :]).then_inc(k_hi_made, 1)

            def fields(i, l):
                ps = slots[i % PSUM_BUFS]
                act.wait_ge(fields_turned, l + 1)
                free_e(act, l)
                nc.scalar.copy(e_hi[:, l % 2, :, :], ps[:].rearrange("p (f b) -> p f b", f=2)).then_inc(e_hi_made, 1)
                nc.scalar.copy(e_pair[0:D, l, :], ps[0:D, 0:B])
                nc.scalar.copy(e_pair[D:P, l, :], ps[D:P, B:2 * B]).then_inc(e_pair_made, 1)

            def double(l):
                act.wait_ge(gather_in[l % GATHER_BUFS], 2 * BT * 16 * (l // GATHER_BUFS + 1))
                if l >= 2:
                    act.wait_ge(fields_turned, l - 1)
                rows = gathered[:, l % GATHER_BUFS, :, :, :].rearrange("p f t d -> p (f t) d")
                nc.scalar.copy(twice[:, l % 2, :, :, :, :].rearrange("p f t h d -> p (f t) h d"),
                               rows.unsqueeze(2).broadcast_to([P, 2 * BT, 2, D])).then_inc(rows_doubled, 1)

            def z_out(kc):
                nc.scalar.copy(z_sb[:, kc, :], z_ps[kc % 2][:]).then_inc(z_copied, 1)

            for i in range(len(order) + LAG):
                for n in split_before.get(i, []):
                    k_hi(n)
                if i < len(order) and order[i][0] == "fields":
                    if order[i][1] == 0:
                        double(0)
                    fields(i, order[i][1])
                    if order[i][1] + 1 < STAGES:
                        double(order[i][1] + 1)
                if i >= LAG:
                    for kc in z_chunks_ended(i - LAG):
                        act.wait_ge(products_summed, product_no[i - LAG] + 1)
                        z_out(kc)
            act.wait_ge(weights_in, 3 * 16)
            for n in range(0, NC1, 2):
                act.wait_ge(h1_summed, n + 1)
                nc.scalar.activation(h1_sb[:, n, :], h_ps(n), ACT.Relu, bias=b1_sb[:, n:n + 1]).then_inc(h1_made, 1)
            act.wait_ge(h2_summed, 1)
            nc.scalar.activation(h2_sb[:, 0, :], h_ps(NC1), ACT.Relu, bias=b2_sb[:, 0:1]).then_inc(h2_made, 1)
            act.wait_ge(y_summed, 1)
            nc.scalar.copy(y_sb, z_ps[0][0:1, :]).then_inc(y_copied, 1)

        @block.vector
        def _(dve):
            nc.vector.memset(select[:], 0.0).then_inc(select_made, 1)
            flat = select[:].rearrange("p s m -> p (s m)")
            dve.wait_ge(select_made, 1)
            nc.vector.memset(flat[0:D, 0:16 * 32:33], 1.0).then_inc(select_made, 1)
            nc.vector.memset(flat[D:P, 16:16 * 32:33], 1.0).then_inc(select_made, 1)
            nc.vector.memset(k_diag[:, CHUNK_COLS:].bitcast(F32), 0.0).then_inc(select_made, 1)

            def k_lo(n):
                dve.wait_ge(k_hi_made, n + 1)
                lo = split_place(n)[D:P, :]
                nc.vector.tensor_tensor(lo, k_raw[D:P, n % RAW_BUFS, :], lo, ALU.subtract).then_inc(k_lo_made, 1)

            def fields_lo(i, l):
                dve.wait_ge(e_pair_made, l + 1)
                nc.vector.tensor_tensor(e_lo[:, l % 2, :, :], slots[i % PSUM_BUFS][:].rearrange("p (f b) -> p f b", f=2),
                                        e_hi[:, l % 2, :, :], ALU.subtract).then_inc(e_lo_made, 1)

            def product(i):
                n, step = product_no[i], order[i]
                ps, to = slots[i % PSUM_BUFS], prod[:, n % PROD_BUFS, :]
                dve.wait_ge(forms_made, n + 1)
                if n >= PROD_BUFS:
                    dve.wait_ge(products_summed, n - PROD_BUFS + 1)
                k = step[2] if step[0] == "block" else step[1]
                dve.wait_ge(e_pair_made, k + 1)
                if step[0] == "block":
                    other = e_pair[:, k, :].unsqueeze(1).broadcast_to([P, 2, B])
                    nc.vector.tensor_tensor(to.rearrange("p (f b) -> p f b", f=2), ps[:].rearrange("p (f b) -> p f b", f=2),
                                            other, ALU.mult).then_inc(products_made, 1)
                else:
                    nc.vector.tensor_tensor(to[0:D, 0:B], ps[0:D, 0:B], e_pair[0:D, k, :],
                                            ALU.mult).then_inc(products_made, 1)

            waiting = None
            for i in range(len(order)):
                for n in split_before.get(i, []):
                    k_lo(n)
                if order[i][0] == "fields":
                    waiting = (i, order[i][1])
                    if i + 1 < len(order) and order[i + 1][1] >= order[i][1]:
                        fields_lo(*waiting)
                        waiting = None
                else:
                    product(i)
                    if waiting:
                        fields_lo(*waiting)
                        waiting = None
            dve.wait_ge(weights_in, 3 * 16)
            for n in range(1, NC1, 2):
                dve.wait_ge(h1_summed, n + 1)
                nc.vector.tensor_scalar(h1_sb[:, n, :], h_ps(n), b1_sb[:, n:n + 1], 0.0, ALU.add,
                                        ALU.max).then_inc(h1_made, 1)
            dve.wait_ge(h2_summed, 2)
            nc.vector.tensor_scalar(h2_sb[:, 1, :], h_ps(NC1 + 1), b2_sb[:, 1:2], 0.0, ALU.add,
                                    ALU.max).then_inc(h2_made, 1)

        @block.tensor
        def _(pe):
            def turn(i, l):
                ps = slots[i % PSUM_BUFS]
                pe.wait_ge(rows_doubled, l + 1)
                free_slot(pe, i)
                for f in (0, 1):
                    for t in range(BT):
                        rows = twice[:, l % 2, f, t, :, :].rearrange("p h d -> p (h d)")
                        last = nc.tensor.transpose(ps[:, f * B + t * P:f * B + (t + 1) * P], rows, ident[:])
                last.then_inc(fields_turned, 1)

            def form(ps, weights, l, f):
                nc.tensor.matmul(ps, weights, e_hi[:, l % 2, f, :], start=True, stop=False)
                return nc.tensor.matmul(ps, weights, e_lo[:, l % 2, f, :], start=False, stop=True)

            def forms(i):
                step, ps = order[i], slots[i % PSUM_BUFS]
                l = step[1]
                free_slot(pe, i)
                pe.wait_ge(e_hi_made, l + 1)
                pe.wait_ge(e_lo_made, l + 1)
                if step[0] == "block":
                    b = blocks.index((l, step[2]))
                    n, at = 1 + b // BLOCKS_PER_CHUNK, b % BLOCKS_PER_CHUNK
                    pe.wait_ge(k_lo_made, n + 1)
                    for f in (0, 1):
                        col = (2 * at + f) * 2 * D
                        last = form(ps[:, f * B:(f + 1) * B], split_place(n)[:, col:col + 2 * D], l, f)
                else:
                    pe.wait_ge(k_lo_made, 1)
                    last = form(ps[:, 0:B], k_diag[:, l * D:(l + 2) * D], l, 1)
                last.then_inc(forms_made, 1)

            def sums(i):
                n, rows = product_no[i], P if order[i][0] == "block" else D
                pe.wait_ge(products_made, n + 1)
                for h in range(tiles_of(order[i])):
                    t = first_tile[i] + h
                    kc, u = t // TILES_PER_CHUNK, t % TILES_PER_CHUNK
                    if kc >= 2 and u == 0:
                        pe.wait_ge(z_copied, kc - 1)
                    g = 32 * (t % 4)
                    last = nc.tensor.matmul(z_ps[kc % 2][g:g + 32, :], select[0:rows, u // 4, :],
                                            prod[0:rows, n % PROD_BUFS, h * B:(h + 1) * B],
                                            start=(u < 4), stop=(u >= TILES_PER_CHUNK - 4), skip_group_check=True)
                last.then_inc(products_summed, 1)

            pe.wait_ge(consts_made, 1)
            pe.wait_ge(select_made, 4)
            for i in range(len(order) + LAG):
                if i < len(order):
                    if order[i][0] == "fields":
                        turn(i, order[i][1])
                    else:
                        forms(i)
                if i >= LAG and order[i - LAG][0] != "fields":
                    sums(i - LAG)

            pe.wait_ge(weights_in, 3 * 16)
            pe.wait_ge(products_made, len(products))
            for kcs in ((0, 1, 2), (3,)):
                pe.wait_ge(z_copied, kcs[-1] + 1)
                for kc in kcs:
                    pe.wait_ge(dense_in[kc], 16 * sum(row // P == kc for _, row in spare_rows))
                for n in range(NC1):
                    for kc in kcs:
                        last = nc.tensor.matmul(h_ps(n), w1_sb[:, kc, n * P:(n + 1) * P], z_sb[:, kc, :],
                                                start=(kc == 0), stop=(kc == KC1 - 1))
                    if kcs[-1] == KC1 - 1:
                        last.then_inc(h1_summed, 1)
            pe.wait_ge(h1_made, NC1)
            for m in range(NC2):
                for kc in range(KC2):
                    last = nc.tensor.matmul(h_ps(NC1 + m), w2_sb[:, kc, m * P:(m + 1) * P], h1_sb[:, kc, :],
                                            start=(kc == 0), stop=(kc == KC2 - 1))
                last.then_inc(h2_summed, 1)
            pe.wait_ge(h2_made, NC2)
            for m in range(NC2):
                last = nc.tensor.matmul(z_ps[0][0:1, :], w3_sb[:, m:m + 1], h2_sb[:, m, :],
                                        start=(m == 0), stop=(m == NC2 - 1))
            last.then_inc(y_summed, 1)


def kernel(**inputs):
    import numpy as np
    import concourse.bacc as bacc
    from concourse.bass_utils import run_bass_kernel_spmd

    arrays = {name: np.ascontiguousarray(a) for name, a in inputs.items()}
    rows, _ = z_layout()
    laid = {f"tbl_{f}": arrays[f"tbl_{f}"] for f in range(FIELDS)}
    laid["ids"] = arrays["ids"]
    laid["dense_t"] = np.ascontiguousarray(arrays["dense_ctx"].T)
    laid["k_pairs"] = np.ascontiguousarray(arrays["L0_rec_kernel"][:, pair_order(), :])
    laid["w1"] = np.ascontiguousarray(arrays["W_top1"][rows])
    laid["w2"] = arrays["W_top2"]
    vectors = [arrays[n].reshape(-1, P) for n in ("b_top1", "b_top2", "W_top3")]
    laid["b1_b2_w3"] = np.ascontiguousarray(np.concatenate(vectors).T)

    nc = bacc.Bacc("TRN2", target_bir_lowering=False, num_devices=1)
    ap = {n: nc.dram_tensor(n, a.shape, mybir.dt.from_np(a.dtype), kind="ExternalInput").ap() for n, a in laid.items()}
    out = nc.dram_tensor("y", (B, 1), F32, kind="ExternalOutput").ap()
    build(nc, ap["dense_t"], ap["ids"], [ap[f"tbl_{f}"] for f in range(FIELDS)], ap["k_pairs"],
          ap["w1"], ap["w2"], ap["b1_b2_w3"], out)
    r = run_bass_kernel_spmd(nc, [laid], core_ids=[0])
    return r.results[0]["y"]
```

```python
from contextlib import ExitStack

import concourse.bass as bass
from concourse import mybir

F32 = mybir.dt.float32
F32R = mybir.dt.float32r
I32 = mybir.dt.int32
ALU = mybir.AluOpType
ACT = mybir.ActivationFunctionType

P = 128
FIELDS = 32
D = 64
B = 512
BT = B // P
DENSE = 16
STAGES = FIELDS // 2
PAIRS = FIELDS * (FIELDS - 1) // 2
H1, H2 = 512, 256
KC1, KC2, NC1, NC2 = 4, H1 // P, H1 // P, H2 // P

DIAG_PAIRS, CHUNK_PAIRS = STAGES, 32
CHUNKS = 1 + (PAIRS - DIAG_PAIRS) // CHUNK_PAIRS
BLOCKS_PER_CHUNK = CHUNK_PAIRS // 4
RAW_BUFS = 2
PARTS_BUFS = 2
SPLIT_BUFS = 6
GATHER_BUFS = 4
PSUM_BUFS = 3
PROD_BUFS = 5
LAG = 2

TILES_PER_CHUNK = 64
BATCH = 4
BATCHES = KC1 * TILES_PER_CHUNK // BATCH


def pair_index(r, c):
    return r * (FIELDS - 1) - r * (r - 1) // 2 + c - r - 1


def pair_order():
    pairs = [pair_index(2 * l, 2 * l + 1) for l in range(STAGES)]
    for l in range(STAGES):
        for k in range(l):
            for c in (2 * l, 2 * l + 1):
                pairs += [pair_index(2 * k, c), pair_index(2 * k + 1, c)]
    return pairs


def chunk_pairs(n):
    return (0, DIAG_PAIRS) if n == 0 else (DIAG_PAIRS + (n - 1) * CHUNK_PAIRS, CHUNK_PAIRS)


def z_row(t, h):
    return P * (t // TILES_PER_CHUNK) + 32 * (t % 4) + 16 * h + (t % TILES_PER_CHUNK) // 4


def steps():
    order = [("fields", 0), ("diagonal", 0), ("fields", 1)]
    for l in range(1, STAGES):
        stage = [("block", l, k) for k in range(l)] + [("diagonal", l)]
        if l + 1 < STAGES:
            stage.insert(len(stage) - 1 - min(max(l - 2, 0), 5), ("fields", l + 1))
        order += stage
    return order


def tiles_of(step):
    return {"fields": 0, "block": 2, "diagonal": 1}[step[0]]


def z_layout():
    rows, spare, t = [0] * (PAIRS + DENSE), [], 0
    for step in steps():
        if step[0] == "block":
            _, l, k = step
            for c in (2 * l, 2 * l + 1):
                for h in (0, 1):
                    rows[z_row(t, h)] = pair_index(2 * k + h, c)
                t += 1
        elif step[0] == "diagonal":
            l = step[1]
            rows[z_row(t, 0)] = pair_index(2 * l, 2 * l + 1)
            rows[z_row(t, 1)] = PAIRS + l
            spare.append((l, z_row(t, 1)))
            t += 1
    return rows, spare


def split_schedule(order):
    before = {0: [0, 1]}
    n = 2
    for l in range(CHUNKS - 2):
        before.setdefault(order.index(("diagonal", l)) + 1, []).append(n)
        n += 1
    assert n == CHUNKS
    return before


def build(nc, dense_t, ids, tables, k_diag_pairs, k_pairs, w1, w2, b1_b2_w3, out):
    order = steps()
    split_before = split_schedule(order)
    _, spare_rows = z_layout()
    products = [i for i, s in enumerate(order) if s[0] != "fields"]
    product_no = {i: n for n, i in enumerate(products)}
    step_of_tile = [i for i, s in enumerate(order) for _ in range(tiles_of(s))]
    last_tile = {i: t for t, i in enumerate(step_of_tile)}
    stage_products = [sum(1 for s in order if s[0] != "fields" and s[1] <= l) for l in range(STAGES)]
    blocks = [(l, k) for l in range(STAGES) for k in range(l)]
    block_product = {(s[1], s[2]): product_no[i] for i, s in enumerate(order) if s[0] == "block"}
    batches_after = {}
    for b in range(BATCHES):
        batches_after.setdefault(step_of_tile[BATCH * (b + 1) - 1] + LAG, []).append(b)
    per_chunk = TILES_PER_CHUNK // BATCH
    z_after = {i: bs[-1] // per_chunk for i, bs in batches_after.items() if (bs[-1] + 1) % per_chunk == 0}

    with ExitStack() as ctx:
        def sb(name, shape, dt=F32):
            return ctx.enter_context(nc.sbuf_tensor(name, shape, dt))

        def sem(name):
            return ctx.enter_context(nc.semaphore(name))

        half = CHUNK_PAIRS // 2 * D
        ids_sb = sb("ids_sb", [P, BT, FIELDS], I32)
        gathered = sb("gathered", [P, GATHER_BUFS, BT, 2, D])
        k_raw = sb("k_raw", [P, RAW_BUFS, half])
        k_parts = sb("k_parts", [P, PARTS_BUFS, 2, half], F32R)
        k_split = sb("k_split", [P, SPLIT_BUFS, 2 * half], F32R)
        k_diag = sb("k_diag", [P, DIAG_PAIRS * D + D], F32R)
        e_pair = sb("e_pair", [P, STAGES, B])
        e_parts = sb("e_parts", [P, 2, 2, B], F32R)
        e_moving = sb("e_moving", [P, 2, 2, 2, B], F32R)
        prod = sb("prod", [P, PROD_BUFS, 2 * B])
        select = sb("select", [P, 16, 32])
        ident = sb("ident", [P, P])
        z_sb = sb("z_sb", [P, KC1, B])
        w1_sb = sb("w1_sb", [P, KC1, H1])
        w2_sb = sb("w2_sb", [P, KC2, H2])
        columns = sb("columns", [P, NC1 + 2 * NC2])
        b1_sb = columns[:, 0:NC1]
        b2_sb = columns[:, NC1:NC1 + NC2]
        w3_sb = columns[:, NC1 + NC2:]
        h1_sb = e_pair[:, 0:NC1, :]
        h2_sb = e_pair[:, NC1:NC1 + NC2, :]
        y_sb = e_pair[0:1, NC1 + NC2, :]

        slots = [ctx.enter_context(nc.psum_tensor(f"slot{i}", [P, 2 * B], F32)) for i in range(PSUM_BUFS)]
        z_ps = [ctx.enter_context(nc.psum_tensor(f"z_ps{i}", [P, B], F32)) for i in range(2)]

        ids_in = sem("ids_in")
        k_raw_in = [sem(f"k_raw_in{i}") for i in range(RAW_BUFS)]
        k_diag_in = sem("k_diag_in")
        k_split_in = [sem(f"k_split_in{i}") for i in range(SPLIT_BUFS)]
        gather_in = [sem(f"gather_in{i}") for i in range(GATHER_BUFS)]
        weights_in = sem("weights_in")
        dense_in = [sem(f"dense_in{kc}") for kc in range(KC1)]
        y_out = sem("y_out")
        zeros_made = sem("zeros_made")
        consts_made = sem("consts_made")
        select_made = sem("select_made")
        k_hi_made = sem("k_hi_made")
        k_lo_made = sem("k_lo_made")
        fields_turned = sem("fields_turned")
        e_hi_made = sem("e_hi_made")
        e_pair_made = sem("e_pair_made")
        e_moved = sem("e_moved")
        e_lo_made = sem("e_lo_made")
        forms_made = sem("forms_made")
        products_made = sem("products_made")
        sums_made = sem("sums_made")
        z_copied = sem("z_copied")
        h1_summed = sem("h1_summed")
        h1_made = sem("h1_made")
        h2_summed = sem("h2_summed")
        h2_made = sem("h2_made")
        y_summed = sem("y_summed")
        y_copied = sem("y_copied")

        def split_place(n):
            return k_split[:, (n - 1) % SPLIT_BUFS, :] if n else k_diag[:, 0:DIAG_PAIRS * D]

        def split_landed(eng, n):
            if n == 0:
                eng.wait_ge(k_diag_in, 64)
            else:
                eng.wait_ge(k_split_in[(n - 1) % SPLIT_BUFS], 64 * ((n - 1) // SPLIT_BUFS + 1))

        def raw(n):
            return k_raw[:, n % RAW_BUFS, 0:chunk_pairs(n)[1] // 2 * D]

        def part(n, which):
            return k_parts[:, n % PARTS_BUFS, which, 0:chunk_pairs(n)[1] // 2 * D]

        def free_slot(eng, i):
            if i < PSUM_BUFS:
                return
            old = order[i - PSUM_BUFS]
            if old[0] == "fields":
                eng.wait_ge(e_pair_made, old[1] + 1)
            else:
                eng.wait_ge(products_made, product_no[i - PSUM_BUFS] + 1)

        def h_ps(n):
            return slots[(len(order) + n // 2) % PSUM_BUFS][:, (n % 2) * B:(n % 2 + 1) * B]

        block = ctx.enter_context(nc.Block())

        @block.sync
        def _(sp):
            def move(to, of):
                return sp.dma_start(to.bitcast(F32), of.bitcast(F32))

            def load(n):
                if n >= RAW_BUFS:
                    sp.wait_ge(k_lo_made, n - RAW_BUFS + 1)
                src = k_diag_pairs if n == 0 else k_pairs[n - 1]
                sp.dma_start(raw(n), src).then_inc(k_raw_in[n % RAW_BUFS], 16)

            def bring_k(n):
                sp.wait_ge(k_lo_made, n + 1)
                if n > SPLIT_BUFS:
                    last = blocks[(n - SPLIT_BUFS) * BLOCKS_PER_CHUNK - 1]
                    sp.wait_ge(forms_made, block_product[last] + 1)
                cols = chunk_pairs(n)[1] // 2 * D
                landed = k_split_in[(n - 1) % SPLIT_BUFS] if n else k_diag_in
                for which in (0, 1):
                    for h in (0, 1):
                        move(split_place(n)[which * D:(which + 1) * D, h * cols:(h + 1) * cols],
                             part(n, which)[h * D:(h + 1) * D, :]).then_inc(landed, 16)

            def dense(kc):
                sp.wait_ge(z_copied, kc + 1)
                for l, row in spare_rows:
                    if row // P == kc:
                        sp.dma_start(z_sb[row % P:row % P + 1, kc, :], dense_t[l:l + 1, :]).then_inc(dense_in[kc], 16)

            sp.dma_start(ids_sb[:], ids.rearrange("(t p) f -> p t f", p=P)).then_inc(ids_in, 16)
            for n in range(RAW_BUFS):
                load(n)
            for i in range(len(order) + LAG):
                for n in split_before.get(i, []):
                    bring_k(n)
                    if n + RAW_BUFS < CHUNKS:
                        load(n + RAW_BUFS)
                if i < len(order) and order[i] == ("diagonal", STAGES - 4):
                    sp.dma_start(w1_sb[:], w1.rearrange("(c p) n -> p c n", p=P)).then_inc(weights_in, 16)
                    sp.dma_start(w2_sb[:], w2.rearrange("(c p) n -> p c n", p=P)).then_inc(weights_in, 16)
                    sp.dma_start(columns[:], b1_b2_w3).then_inc(weights_in, 16)
                if i in z_after:
                    dense(z_after[i])
            sp.wait_ge(y_copied, 1)
            sp.dma_start(out.rearrange("b o -> o b"), y_sb).then_inc(y_out, 16)
            sp.wait_ge(y_out, 16)

        @block.gpsimd
        def _(pool):
            nc.gpsimd.memset(ident[:], 0.0).then_inc(zeros_made, 1)
            pool.wait_ge(zeros_made, 1)
            nc.gpsimd.affine_select(out=ident[:], in_=ident[:], compare_op=ALU.not_equal, fill=1.0, base=0,
                                    pattern=[[-1, P]], channel_multiplier=1).then_inc(consts_made, 1)
            pool.wait_ge(ids_in, 16)
            for l in range(STAGES):
                if l >= GATHER_BUFS:
                    pool.wait_ge(fields_turned, l - GATHER_BUFS + 1)
                for f in (0, 1):
                    for t in range(BT):
                        field = 2 * l + f
                        nc.gpsimd.indirect_dma_start(
                            gathered[:, l % GATHER_BUFS, t, f, :], None, tables[field],
                            bass.IndirectOffsetOnAxis(ap=ids_sb[:, t, field:field + 1], axis=0),
                        ).then_inc(gather_in[l % GATHER_BUFS], 16)

        @block.scalar
        def _(act):
            def k_hi(n):
                act.wait_ge(k_raw_in[n % RAW_BUFS], 16 * (n // RAW_BUFS + 1))
                if n >= PARTS_BUFS:
                    split_landed(act, n - PARTS_BUFS)
                nc.scalar.copy(part(n, 0), raw(n)).then_inc(k_hi_made, 1)

            def fields(i, l):
                ps = slots[i % PSUM_BUFS]
                act.wait_ge(fields_turned, l + 1)
                nc.scalar.copy(e_parts[:, l % 2, 0, :], ps[:, 0:B]).then_inc(e_hi_made, 1)
                nc.scalar.copy(e_pair[:, l, :], ps[:, 0:B]).then_inc(e_pair_made, 1)
                act.wait_ge(e_hi_made, l + 1)
                if l >= 2:
                    act.wait_ge(forms_made, stage_products[l - 2])
                for which in (0, 1):
                    if which == 1:
                        act.wait_ge(e_lo_made, l + 1)
                    for f in (0, 1):
                        for h in (0, 1):
                            nc.scalar.copy(e_moving[h * D:(h + 1) * D, l % 2, f, which, :],
                                           e_parts[f * D:(f + 1) * D, l % 2, which, :]).then_inc(e_moved, 1)

            for i in range(len(order) + LAG):
                for n in split_before.get(i, []):
                    k_hi(n)
                if i < len(order) and order[i][0] == "fields":
                    fields(i, order[i][1])
                if i in z_after:
                    kc = z_after[i]
                    act.wait_ge(sums_made, (kc + 1) * per_chunk)
                    nc.scalar.copy(z_sb[:, kc, :], z_ps[kc % 2][:]).then_inc(z_copied, 1)
            act.wait_ge(weights_in, 3 * 16)
            for n in range(0, NC1, 2):
                act.wait_ge(h1_summed, n + 1)
                nc.scalar.activation(h1_sb[:, n, :], h_ps(n), ACT.Relu, bias=b1_sb[:, n:n + 1]).then_inc(h1_made, 1)
            act.wait_ge(h2_summed, 1)
            nc.scalar.activation(h2_sb[:, 0, :], h_ps(NC1), ACT.Relu, bias=b2_sb[:, 0:1]).then_inc(h2_made, 1)
            act.wait_ge(y_summed, 1)
            nc.scalar.copy(y_sb, z_ps[0][0:1, :]).then_inc(y_copied, 1)

        @block.vector
        def _(dve):
            nc.vector.memset(select[:], 0.0).then_inc(select_made, 1)
            flat = select[:].rearrange("p s m -> p (s m)")
            dve.wait_ge(select_made, 1)
            nc.vector.memset(flat[0:D, 0:16 * 32:33], 1.0).then_inc(select_made, 1)
            nc.vector.memset(flat[D:P, 16:16 * 32:33], 1.0).then_inc(select_made, 1)
            nc.vector.memset(k_diag[:, DIAG_PAIRS * D:].bitcast(F32), 0.0).then_inc(select_made, 1)

            def k_lo(n):
                dve.wait_ge(k_hi_made, n + 1)
                nc.vector.tensor_tensor(part(n, 1), raw(n), part(n, 0), ALU.subtract).then_inc(k_lo_made, 1)

            def fields_lo(l):
                dve.wait_ge(e_pair_made, l + 1)
                if l >= 2:
                    dve.wait_ge(e_moved, 8 * (l - 1))
                nc.vector.tensor_tensor(e_parts[:, l % 2, 1, :], e_pair[:, l, :], e_parts[:, l % 2, 0, :],
                                        ALU.subtract).then_inc(e_lo_made, 1)

            def product(i):
                n, step = product_no[i], order[i]
                ps, to = slots[i % PSUM_BUFS], prod[:, n % PROD_BUFS, :]
                dve.wait_ge(forms_made, n + 1)
                if n >= PROD_BUFS:
                    dve.wait_ge(sums_made, last_tile[products[n - PROD_BUFS]] // BATCH + 1)
                k = step[2] if step[0] == "block" else step[1]
                dve.wait_ge(e_pair_made, k + 1)
                if step[0] == "block":
                    other = e_pair[:, k, :].unsqueeze(1).broadcast_to([P, 2, B])
                    nc.vector.tensor_tensor(to.rearrange("p (f b) -> p f b", f=2), ps[:].rearrange("p (f b) -> p f b", f=2),
                                            other, ALU.mult).then_inc(products_made, 1)
                else:
                    nc.vector.tensor_tensor(to[0:D, 0:B], ps[0:D, 0:B], e_pair[0:D, k, :],
                                            ALU.mult).then_inc(products_made, 1)

            waiting = None
            for i in range(len(order)):
                for n in split_before.get(i, []):
                    k_lo(n)
                if order[i][0] == "fields":
                    waiting = order[i][1]
                    if order[i + 1][1] >= waiting:
                        fields_lo(waiting)
                        waiting = None
                else:
                    product(i)
                    if waiting is not None:
                        fields_lo(waiting)
                        waiting = None
            dve.wait_ge(weights_in, 3 * 16)
            for n in range(1, NC1, 2):
                dve.wait_ge(h1_summed, n + 1)
                nc.vector.tensor_scalar(h1_sb[:, n, :], h_ps(n), b1_sb[:, n:n + 1], 0.0, ALU.add,
                                        ALU.max).then_inc(h1_made, 1)
            dve.wait_ge(h2_summed, 2)
            nc.vector.tensor_scalar(h2_sb[:, 1, :], h_ps(NC1 + 1), b2_sb[:, 1:2], 0.0, ALU.add,
                                    ALU.max).then_inc(h2_made, 1)

        @block.tensor
        def _(pe):
            def turn(i, l):
                pe.wait_ge(gather_in[l % GATHER_BUFS], 2 * BT * 16 * (l // GATHER_BUFS + 1))
                free_slot(pe, i)
                for t in range(BT):
                    rows = gathered[:, l % GATHER_BUFS, t, :, :].rearrange("p f d -> p (f d)")
                    last = nc.tensor.transpose(slots[i % PSUM_BUFS][:, t * P:(t + 1) * P], rows, ident[:])
                last.then_inc(fields_turned, 1)

            def form(ps, weights, l, f):
                nc.tensor.matmul(ps, weights, e_moving[:, l % 2, f, 0, :], start=True, stop=False)
                return nc.tensor.matmul(ps, weights, e_moving[:, l % 2, f, 1, :], start=False, stop=True)

            def forms(i):
                step, ps = order[i], slots[i % PSUM_BUFS]
                l = step[1]
                free_slot(pe, i)
                pe.wait_ge(e_moved, 8 * (l + 1))
                if step[0] == "block":
                    b = blocks.index((l, step[2]))
                    n, at = 1 + b // BLOCKS_PER_CHUNK, b % BLOCKS_PER_CHUNK
                    split_landed(pe, n)
                    for f in (0, 1):
                        col = (2 * at + f) * 2 * D
                        last = form(ps[:, f * B:(f + 1) * B], split_place(n)[:, col:col + 2 * D], l, f)
                else:
                    split_landed(pe, 0)
                    last = form(ps[:, 0:B], k_diag[:, l * D:(l + 2) * D], l, 1)
                last.then_inc(forms_made, 1)

            def sums(b):
                pe.wait_ge(products_made, product_no[step_of_tile[BATCH * (b + 1) - 1]] + 1)
                kc, u = b // per_chunk, b % per_chunk
                if kc >= 2 and u == 0:
                    pe.wait_ge(z_copied, kc - 1)
                for t in range(BATCH * b, BATCH * (b + 1)):
                    i = step_of_tile[t]
                    h = t - (last_tile[i] + 1 - tiles_of(order[i]))
                    rows = P if order[i][0] == "block" else D
                    g = 32 * (t % BATCH)
                    last = nc.tensor.matmul(z_ps[kc % 2][g:g + 32, :], select[0:rows, u, :],
                                            prod[0:rows, product_no[i] % PROD_BUFS, h * B:(h + 1) * B],
                                            start=(u == 0), stop=(u == per_chunk - 1), skip_group_check=True)
                last.then_inc(sums_made, 1)

            pe.wait_ge(consts_made, 1)
            pe.wait_ge(select_made, 4)
            for i in range(len(order) + LAG):
                if i < len(order):
                    if order[i][0] == "fields":
                        turn(i, order[i][1])
                    else:
                        forms(i)
                for b in batches_after.get(i, []):
                    sums(b)

            pe.wait_ge(weights_in, 3 * 16)
            pe.wait_ge(products_made, len(products))
            for kcs in ((0, 1, 2), (3,)):
                pe.wait_ge(z_copied, kcs[-1] + 1)
                for kc in kcs:
                    pe.wait_ge(dense_in[kc], 16 * sum(row // P == kc for _, row in spare_rows))
                for n in range(NC1):
                    for kc in kcs:
                        last = nc.tensor.matmul(h_ps(n), w1_sb[:, kc, n * P:(n + 1) * P], z_sb[:, kc, :],
                                                start=(kc == 0), stop=(kc == KC1 - 1))
                    if kcs[-1] == KC1 - 1:
                        last.then_inc(h1_summed, 1)
            pe.wait_ge(h1_made, NC1)
            for m in range(NC2):
                for kc in range(KC2):
                    last = nc.tensor.matmul(h_ps(NC1 + m), w2_sb[:, kc, m * P:(m + 1) * P], h1_sb[:, kc, :],
                                            start=(kc == 0), stop=(kc == KC2 - 1))
                last.then_inc(h2_summed, 1)
            pe.wait_ge(h2_made, NC2)
            for m in range(NC2):
                last = nc.tensor.matmul(z_ps[0][0:1, :], w3_sb[:, m:m + 1], h2_sb[:, m, :],
                                        start=(m == 0), stop=(m == NC2 - 1))
            last.then_inc(y_summed, 1)


def kernel(**inputs):
    import numpy as np
    import concourse.bacc as bacc
    from concourse.bass_utils import run_bass_kernel_spmd

    arrays = {name: np.ascontiguousarray(a) for name, a in inputs.items()}
    laid = {f"tbl_{f}": arrays[f"tbl_{f}"] for f in range(FIELDS)}
    laid["ids"] = arrays["ids"]
    laid["dense_t"] = np.ascontiguousarray(arrays["dense_ctx"].T)
    k = arrays["L0_rec_kernel"][:, pair_order(), :]

    def chunks(pairs, count):
        return np.ascontiguousarray(pairs.reshape(D, count, 2, -1).transpose(1, 2, 0, 3).reshape(count, P, -1))

    laid["k_diag_pairs"] = chunks(k[:, :DIAG_PAIRS], 1)[0]
    laid["k_pairs"] = chunks(k[:, DIAG_PAIRS:], CHUNKS - 1)
    laid["w1"] = np.ascontiguousarray(arrays["W_top1"][z_layout()[0]])
    laid["w2"] = arrays["W_top2"]
    vectors = [arrays[n].reshape(-1, P) for n in ("b_top1", "b_top2", "W_top3")]
    laid["b1_b2_w3"] = np.ascontiguousarray(np.concatenate(vectors).T)

    nc = bacc.Bacc("TRN2", target_bir_lowering=False, num_devices=1)
    ap = {n: nc.dram_tensor(n, a.shape, mybir.dt.from_np(a.dtype), kind="ExternalInput").ap() for n, a in laid.items()}
    out = nc.dram_tensor("y", (B, 1), F32, kind="ExternalOutput").ap()
    build(nc, ap["dense_t"], ap["ids"], [ap[f"tbl_{f}"] for f in range(FIELDS)], ap["k_diag_pairs"], ap["k_pairs"],
          ap["w1"], ap["w2"], ap["b1_b2_w3"], out)
    r = run_bass_kernel_spmd(nc, [laid], core_ids=[0])
    return r.results[0]["y"]
```

```python
from contextlib import ExitStack

import concourse.bass as bass
from concourse import mybir

F32 = mybir.dt.float32
F32R = mybir.dt.float32r
I32 = mybir.dt.int32
ALU = mybir.AluOpType
ACT = mybir.ActivationFunctionType

P = 128
FIELDS = 32
D = 64
B = 512
BT = B // P
DENSE = 16
STAGES = FIELDS // 2
PAIRS = FIELDS * (FIELDS - 1) // 2
ONE_HOT_STAGES = (0, 2)
SMALL_FIELDS = (1, 3, 4, 7)
SMALL_ROWS, SMALL_P = 1000, 125
SMALL_C = SMALL_ROWS // SMALL_P
H1, H2 = 512, 256
KC1, KC2, NC1, NC2 = 4, H1 // P, H1 // P, H2 // P

DIAG_PAIRS, CHUNK_PAIRS = STAGES, 32
CHUNKS = 1 + (PAIRS - DIAG_PAIRS) // CHUNK_PAIRS
BLOCKS_PER_CHUNK = CHUNK_PAIRS // 4
RAW_BUFS = 2
PARTS_BUFS = 2
SPLIT_BUFS = 6
GATHER_BUFS = 4
PSUM_BUFS = 3
PROD_BUFS = 5
FIELDS_AHEAD = 9
LO_AT_ONCE = 8
LAG = 2

TILES_PER_CHUNK = 64
ONE_HOT_BUFS = 8
TABLE_BUFS = 4
BATCH = 4
BATCHES = KC1 * TILES_PER_CHUNK // BATCH


def field_order():
    small, rest = iter(SMALL_FIELDS), iter(f for f in range(FIELDS) if f not in SMALL_FIELDS)
    return [next(small if place // 2 in ONE_HOT_STAGES else rest) for place in range(FIELDS)]


def pair_of(p, q):
    fields = field_order()
    r, c = sorted((fields[p], fields[q]))
    return r * (FIELDS - 1) - r * (r - 1) // 2 + c - r - 1, r == fields[q]


def pair_order():
    pairs = [pair_of(2 * l, 2 * l + 1) for l in range(STAGES)]
    for l in range(STAGES):
        for k in range(l):
            for c in (2 * l, 2 * l + 1):
                pairs += [pair_of(2 * k, c), pair_of(2 * k + 1, c)]
    return pairs


def chunk_pairs(n):
    return (0, DIAG_PAIRS) if n == 0 else (DIAG_PAIRS + (n - 1) * CHUNK_PAIRS, CHUNK_PAIRS)


def z_row(t, h):
    return P * (t // TILES_PER_CHUNK) + 32 * (t % 4) + 16 * h + (t % TILES_PER_CHUNK) // 4


def steps():
    order = [("fields", 0)]
    for l in range(STAGES):
        stage = [("block", l, k) for k in range(l)] + [("diagonal", l)]
        if l < STAGES - 1:
            stage.insert(max(0, len(stage) - FIELDS_AHEAD), ("fields", l + 1))
        order += stage
    return order


def tiles_of(step):
    return {"fields": 0, "block": 2, "diagonal": 1}[step[0]]


def z_layout():
    rows, spare, t = [0] * (PAIRS + DENSE), [], 0
    for step in steps():
        if step[0] == "block":
            _, l, k = step
            for c in (2 * l, 2 * l + 1):
                for h in (0, 1):
                    rows[z_row(t, h)] = pair_of(2 * k + h, c)[0]
                t += 1
        elif step[0] == "diagonal":
            l = step[1]
            rows[z_row(t, 0)] = pair_of(2 * l, 2 * l + 1)[0]
            rows[z_row(t, 1)] = PAIRS + l
            spare.append((l, z_row(t, 1)))
            t += 1
    return rows, spare


def split_schedule(order):
    before = {0: [0, 1]}
    for n in range(2, CHUNKS):
        stage = n - 1 if n < CHUNKS - 2 else n - 2
        before.setdefault(order.index(("diagonal", stage)) + 1, []).append(n)
    return before


def one_hot_schedule(order):
    at = order.index(("fields", 1))
    return {0: [(0, 0), (0, 1)], at: [(1, 0)], at + 1: [(1, 1)]}


def build(nc, dense_t, ids, small_ids, row_numbers, tables, k_diag_pairs, k_pairs, w1, w2, b1_b2_w3, out):
    order = steps()
    split_before = split_schedule(order)
    one_hot_before = one_hot_schedule(order)
    gather_stages = [l for l in range(STAGES) if l not in ONE_HOT_STAGES]
    gather_no = {l: g for g, l in enumerate(gather_stages)}
    one_hot_no = {l: s for s, l in enumerate(ONE_HOT_STAGES)}
    fields_at = field_order()
    _, spare_rows = z_layout()
    products = [i for i, s in enumerate(order) if s[0] != "fields"]
    product_no = {i: n for n, i in enumerate(products)}
    step_of_tile = [i for i, s in enumerate(order) for _ in range(tiles_of(s))]
    last_tile = {i: t for t, i in enumerate(step_of_tile)}
    stage_products = [sum(1 for s in order if s[0] != "fields" and s[1] <= l) for l in range(STAGES)]
    blocks = [(l, k) for l in range(STAGES) for k in range(l)]
    block_product = {(s[1], s[2]): product_no[i] for i, s in enumerate(order) if s[0] == "block"}
    batches_after = {}
    for b in range(BATCHES):
        batches_after.setdefault(step_of_tile[BATCH * (b + 1) - 1] + LAG, []).append(b)
    per_chunk = TILES_PER_CHUNK // BATCH
    z_after = {i: bs[-1] // per_chunk for i, bs in batches_after.items() if (bs[-1] + 1) % per_chunk == 0}

    with ExitStack() as ctx:
        def sb(name, shape, dt=F32):
            return ctx.enter_context(nc.sbuf_tensor(name, shape, dt))

        def sem(name):
            return ctx.enter_context(nc.semaphore(name))

        half = CHUNK_PAIRS // 2 * D
        ids_sb = sb("ids_sb", [P, BT, FIELDS], I32)
        gathered = sb("gathered", [P, GATHER_BUFS, BT, 2, D])
        k_raw = sb("k_raw", [P, RAW_BUFS, half])
        k_parts = sb("k_parts", [P, PARTS_BUFS, 2, half], F32R)
        k_split = sb("k_split", [P, SPLIT_BUFS, 2 * half], F32R)
        k_diag = sb("k_diag", [P, DIAG_PAIRS * D + D], F32R)
        e_pair = sb("e_pair", [P, STAGES, B])
        e_parts = sb("e_parts", [P, 2, 2, B], F32R)
        e_moving = sb("e_moving", [P, 2, 2, 2, B], F32R)
        prod = sb("prod", [P, PROD_BUFS, 2 * B])
        select = sb("select", [P, 16, 32])
        ident = sb("ident", [P, P])
        one_hot = sb("one_hot", [P, ONE_HOT_BUFS, B], F32R)
        table_parts = k_split[:, SPLIT_BUFS - TABLE_BUFS // 2:, :].rearrange("p a (f n) -> p (a f) n", f=2)
        row_no = sb("row_no", [P, SMALL_C])
        shared = sb("shared", [P, max(KC1 * B + KC1 * H1 + KC2 * H2, 2 * len(SMALL_FIELDS) * B)])
        z_sb = shared[:, 0:KC1 * B].rearrange("p (c b) -> p c b", c=KC1)
        w1_sb = shared[:, KC1 * B:KC1 * (B + H1)].rearrange("p (c n) -> p c n", c=KC1)
        w2_sb = shared[:, KC1 * (B + H1):KC1 * (B + H1) + KC2 * H2].rearrange("p (c n) -> p c n", c=KC2)
        small_raw = shared[:, 0:len(SMALL_FIELDS) * B].rearrange("p (f n) -> p f n", n=B)
        ids_all = shared[:, len(SMALL_FIELDS) * B:2 * len(SMALL_FIELDS) * B].bitcast(I32).rearrange(
            "p (f b) -> p f b", b=B)
        columns = sb("columns", [P, NC1 + 2 * NC2])
        b1_sb = columns[:, 0:NC1]
        b2_sb = columns[:, NC1:NC1 + NC2]
        w3_sb = columns[:, NC1 + NC2:]
        h1_sb = e_pair[:, 0:NC1, :]
        h2_sb = e_pair[:, NC1:NC1 + NC2, :]
        y_sb = e_pair[0:1, NC1 + NC2, :]

        slots = [ctx.enter_context(nc.psum_tensor(f"slot{i}", [P, 2 * B], F32)) for i in range(PSUM_BUFS)]
        z_ps = [ctx.enter_context(nc.psum_tensor(f"z_ps{i}", [P, B], F32)) for i in range(2)]

        ids_in = sem("ids_in")
        k_raw_in = [sem(f"k_raw_in{i}") for i in range(RAW_BUFS)]
        k_diag_in = sem("k_diag_in")
        k_split_in = [sem(f"k_split_in{i}") for i in range(SPLIT_BUFS)]
        row_no_in = sem("row_no_in")
        small_in = [sem(f"small_in{s}") for s in range(len(ONE_HOT_STAGES))]
        gather_in = [sem(f"gather_in{i}") for i in range(GATHER_BUFS)]
        weights_in = sem("weights_in")
        dense_in = [sem(f"dense_in{kc}") for kc in range(KC1)]
        y_out = sem("y_out")
        zeros_made = sem("zeros_made")
        consts_made = sem("consts_made")
        select_made = sem("select_made")
        k_hi_made = sem("k_hi_made")
        k_lo_made = sem("k_lo_made")
        table_hi_made = sem("table_hi_made")
        table_lo_made = sem("table_lo_made")
        one_hots_made = sem("one_hots_made")
        one_hots_used = sem("one_hots_used")
        fields_turned = sem("fields_turned")
        e_hi_made = sem("e_hi_made")
        e_pair_made = sem("e_pair_made")
        e_sum_made = sem("e_sum_made")
        e_moved = sem("e_moved")
        e_lo_made = sem("e_lo_made")
        forms_made = sem("forms_made")
        products_made = sem("products_made")
        sums_made = sem("sums_made")
        z_copied = sem("z_copied")
        h1_summed = sem("h1_summed")
        h1_made = [sem(f"h1_made{i}") for i in range(2)]
        h2_summed = sem("h2_summed")
        h2_made = [sem(f"h2_made{i}") for i in range(2)]
        y_summed = sem("y_summed")
        y_copied = sem("y_copied")

        def split_place(n):
            return k_split[:, (n - 1) % SPLIT_BUFS, :] if n else k_diag[:, 0:DIAG_PAIRS * D]

        def split_landed(eng, n):
            if n == 0:
                eng.wait_ge(k_diag_in, 64)
            else:
                eng.wait_ge(k_split_in[(n - 1) % SPLIT_BUFS], 64 * ((n - 1) // SPLIT_BUFS + 1))

        def raw(n):
            return k_raw[:, n % RAW_BUFS, 0:chunk_pairs(n)[1] // 2 * D]

        def part(n, which):
            return k_parts[:, n % PARTS_BUFS, which, 0:chunk_pairs(n)[1] // 2 * D]

        def pair_made(eng, l):
            if l in one_hot_no:
                eng.wait_ge(e_sum_made, 2 * (one_hot_no[l] + 1))
            else:
                eng.wait_ge(e_pair_made, gather_no[l] + 1)

        def free_slot(eng, i):
            if i < PSUM_BUFS:
                return
            old = order[i - PSUM_BUFS]
            if old[0] != "fields":
                eng.wait_ge(products_made, product_no[i - PSUM_BUFS] + 1)
            elif old[1] in one_hot_no:
                eng.wait_ge(e_moved, 8 * (old[1] + 1))
            else:
                pair_made(eng, old[1])

        def h_ps(n):
            return slots[(len(order) + n // 2) % PSUM_BUFS][:, (n % 2) * B:(n % 2 + 1) * B]

        block = ctx.enter_context(nc.Block())

        @block.sync
        def _(sp):
            def move(to, of):
                return sp.dma_start(to.bitcast(F32), of.bitcast(F32))

            def load(n):
                if n >= RAW_BUFS:
                    sp.wait_ge(k_lo_made, n - RAW_BUFS + 1)
                src = k_diag_pairs if n == 0 else k_pairs[n - 1]
                sp.dma_start(raw(n), src).then_inc(k_raw_in[n % RAW_BUFS], 16)

            def bring_k(n):
                sp.wait_ge(k_lo_made, n + 1)
                if SPLIT_BUFS - TABLE_BUFS // 2 < n <= SPLIT_BUFS:
                    sp.wait_ge(one_hots_used, SMALL_C * len(SMALL_FIELDS))
                if n > SPLIT_BUFS:
                    last = blocks[(n - SPLIT_BUFS) * BLOCKS_PER_CHUNK - 1]
                    sp.wait_ge(forms_made, block_product[last] + 1)
                cols = chunk_pairs(n)[1] // 2 * D
                landed = k_split_in[(n - 1) % SPLIT_BUFS] if n else k_diag_in
                for which in (0, 1):
                    for h in (0, 1):
                        move(split_place(n)[which * D:(which + 1) * D, h * cols:(h + 1) * cols],
                             part(n, which)[h * D:(h + 1) * D, :]).then_inc(landed, 16)

            def dense(kc):
                sp.wait_ge(z_copied, kc + 1)
                for l, row in spare_rows:
                    if row // P == kc:
                        sp.dma_start(z_sb[row % P:row % P + 1, kc, :], dense_t[l:l + 1, :]).then_inc(dense_in[kc], 16)

            def small_loads(s):
                sp.dma_start(ids_all[:, 2 * s:2 * s + 2, :].rearrange("p f b -> p (f b)"),
                             small_ids[s:s + 1, :].broadcast_to([P, 2 * B])).then_inc(small_in[s], 16)
                for n in (2 * s, 2 * s + 1):
                    sp.dma_start(small_raw[0:SMALL_P, n, :], tables[SMALL_FIELDS[n]].rearrange(
                        "(p c) d -> p (c d)", c=SMALL_C)).then_inc(small_in[s], 16)

            small_loads(0)
            sp.dma_start(ids_sb[:], ids.rearrange("(t p) f -> p t f", p=P)).then_inc(ids_in, 16)
            sp.dma_start(row_no[0:SMALL_P, :], row_numbers).then_inc(row_no_in, 16)
            for n in range(RAW_BUFS):
                load(n)
            for s in range(1, len(ONE_HOT_STAGES)):
                small_loads(s)
            for i in range(len(order) + LAG):
                for n in split_before.get(i, []):
                    bring_k(n)
                    if n + RAW_BUFS < CHUNKS:
                        load(n + RAW_BUFS)
                if i < len(order) and order[i] == ("diagonal", STAGES - 4):
                    sp.dma_start(w1_sb, w1.rearrange("(c p) n -> p c n", p=P)).then_inc(weights_in, 16)
                    sp.dma_start(w2_sb, w2.rearrange("(c p) n -> p c n", p=P)).then_inc(weights_in, 16)
                    sp.dma_start(columns[:], b1_b2_w3).then_inc(weights_in, 16)
                if i in z_after:
                    dense(z_after[i])
            sp.wait_ge(y_copied, 1)
            sp.dma_start(out.rearrange("b o -> o b"), y_sb).then_inc(y_out, 16)
            sp.wait_ge(y_out, 16)

        @block.gpsimd
        def _(pool):
            nc.gpsimd.memset(ident[:], 0.0).then_inc(zeros_made, 1)
            pool.wait_ge(zeros_made, 1)
            nc.gpsimd.affine_select(out=ident[:], in_=ident[:], compare_op=ALU.not_equal, fill=1.0, base=0,
                                    pattern=[[-1, P]], channel_multiplier=1).then_inc(consts_made, 1)
            pool.wait_ge(ids_in, 16)
            for g, l in enumerate(gather_stages):
                if g >= GATHER_BUFS:
                    pool.wait_ge(fields_turned, g - GATHER_BUFS + 1)
                for f in (0, 1):
                    for t in range(BT):
                        field = fields_at[2 * l + f]
                        nc.gpsimd.indirect_dma_start(
                            gathered[:, g % GATHER_BUFS, t, f, :], None, tables[field],
                            bass.IndirectOffsetOnAxis(ap=ids_sb[:, t, field:field + 1], axis=0),
                        ).then_inc(gather_in[g % GATHER_BUFS], 16)

        @block.scalar
        def _(act):
            def k_hi(n):
                act.wait_ge(k_raw_in[n % RAW_BUFS], 16 * (n // RAW_BUFS + 1))
                if n >= PARTS_BUFS:
                    split_landed(act, n - PARTS_BUFS)
                nc.scalar.copy(part(n, 0), raw(n)).then_inc(k_hi_made, 1)

            def table_hi(s, f):
                n = 2 * s + f
                act.wait_ge(small_in[s], 3 * 16)
                if n >= TABLE_BUFS:
                    act.wait_ge(one_hots_used, SMALL_C * (n - TABLE_BUFS + 1))
                to = table_parts[0:SMALL_P, n % TABLE_BUFS, :].rearrange("p (c w d) -> p c w d", w=2, d=D)[:, :, 0, :]
                nc.scalar.copy(to, small_raw[0:SMALL_P, n, :].rearrange("p (c d) -> p c d", d=D)).then_inc(
                    table_hi_made, 1)

            def moving_free(l):
                if l >= 2:
                    act.wait_ge(forms_made, stage_products[l - 2])
                if l - 2 in one_hot_no:
                    pair_made(act, l - 2)

            def one_hot_fields(i, l):
                moving_free(l)
                for f in (0, 1):
                    act.wait_ge(one_hots_used, SMALL_C * (2 * one_hot_no[l] + f + 1))
                    for which in (0, 1):
                        for h in (0, 1):
                            nc.scalar.copy(e_moving[h * D:(h + 1) * D, l % 2, f, which, :],
                                           slots[i % PSUM_BUFS][which * D:(which + 1) * D, f * B:(f + 1) * B],
                                           ).then_inc(e_moved, 1)

            def fields(i, l):
                ps, g = slots[i % PSUM_BUFS], gather_no[l]
                act.wait_ge(fields_turned, g + 1)
                nc.scalar.copy(e_parts[:, g % 2, 0, :], ps[:, 0:B]).then_inc(e_hi_made, 1)
                nc.scalar.copy(e_pair[:, l, :], ps[:, 0:B]).then_inc(e_pair_made, 1)
                act.wait_ge(e_hi_made, g + 1)
                moving_free(l)
                for which in (0, 1):
                    if which == 1:
                        act.wait_ge(e_lo_made, g + 1)
                    for f in (0, 1):
                        for h in (0, 1):
                            nc.scalar.copy(e_moving[h * D:(h + 1) * D, l % 2, f, which, :],
                                           e_parts[f * D:(f + 1) * D, g % 2, which, :]).then_inc(e_moved, 1)

            for s in range(len(ONE_HOT_STAGES)):
                for f in (0, 1):
                    table_hi(s, f)
            for i in range(len(order) + LAG):
                for n in split_before.get(i, []):
                    k_hi(n)
                if i < len(order) and order[i][0] == "fields":
                    (one_hot_fields if order[i][1] in one_hot_no else fields)(i, order[i][1])
                if i in z_after:
                    kc = z_after[i]
                    act.wait_ge(sums_made, (kc + 1) * per_chunk)
                    nc.scalar.copy(z_sb[:, kc, :], z_ps[kc % 2][:]).then_inc(z_copied, 1)
            act.wait_ge(weights_in, 3 * 16)
            for n in range(0, NC1, 2):
                act.wait_ge(h1_summed, n + 1)
                nc.scalar.activation(h1_sb[:, n, :], h_ps(n), ACT.Relu, bias=b1_sb[:, n:n + 1]).then_inc(h1_made[0], 1)
            act.wait_ge(h2_summed, 1)
            nc.scalar.activation(h2_sb[:, 0, :], h_ps(NC1), ACT.Relu, bias=b2_sb[:, 0:1]).then_inc(h2_made[0], 1)
            act.wait_ge(y_summed, 1)
            nc.scalar.copy(y_sb, z_ps[0][0:1, :]).then_inc(y_copied, 1)

        @block.vector
        def _(dve):
            nc.vector.memset(select[:], 0.0).then_inc(select_made, 1)
            flat = select[:].rearrange("p s m -> p (s m)")
            dve.wait_ge(select_made, 1)
            nc.vector.memset(flat[0:D, 0:16 * 32:33], 1.0).then_inc(select_made, 1)
            nc.vector.memset(flat[D:P, 16:16 * 32:33], 1.0).then_inc(select_made, 1)
            nc.vector.memset(k_diag[:, DIAG_PAIRS * D:].bitcast(F32), 0.0).then_inc(select_made, 1)

            def k_lo(n):
                dve.wait_ge(k_hi_made, n + 1)
                nc.vector.tensor_tensor(part(n, 1), raw(n), part(n, 0), ALU.subtract).then_inc(k_lo_made, 1)

            def one_hots(s, f):
                n = 2 * s + f
                dve.wait_ge(table_hi_made, n + 1)
                parts = table_parts[0:SMALL_P, n % TABLE_BUFS, :].rearrange("p (c w d) -> p c w d", w=2, d=D)
                raw = small_raw[0:SMALL_P, n, :].rearrange("p (c d) -> p c d", d=D)
                nc.vector.tensor_tensor(parts[:, :, 1, :], raw, parts[:, :, 0, :],
                                        ALU.subtract).then_inc(table_lo_made, 1)
                if n == 0:
                    dve.wait_ge(row_no_in, 16)
                for m in range(SMALL_C * n, SMALL_C * (n + 1)):
                    if m >= ONE_HOT_BUFS:
                        dve.wait_ge(one_hots_used, m - ONE_HOT_BUFS + 1)
                    c = m % SMALL_C
                    nc.vector.tensor_scalar(one_hot[0:SMALL_P, m % ONE_HOT_BUFS, :], ids_all[0:SMALL_P, n, :],
                                            row_no[0:SMALL_P, c:c + 1], None, ALU.is_equal).then_inc(one_hots_made, 1)

            def one_hot_sum(l):
                dve.wait_ge(e_moved, 8 * (l + 1))
                for f in (0, 1):
                    parts = e_moving[f * D:(f + 1) * D, l % 2, f, :, :]
                    nc.vector.tensor_tensor(e_pair[f * D:(f + 1) * D, l, :], parts[:, 0, :], parts[:, 1, :],
                                            ALU.add).then_inc(e_sum_made, 1)

            def fields_lo(l):
                g = gather_no[l]
                pair_made(dve, l)
                if g >= 2:
                    dve.wait_ge(e_moved, 8 * (gather_stages[g - 2] + 1))
                nc.vector.tensor_tensor(e_parts[:, g % 2, 1, :], e_pair[:, l, :], e_parts[:, g % 2, 0, :],
                                        ALU.subtract).then_inc(e_lo_made, 1)

            def product(i):
                n, step = product_no[i], order[i]
                ps, to = slots[i % PSUM_BUFS], prod[:, n % PROD_BUFS, :]
                dve.wait_ge(forms_made, n + 1)
                if n >= PROD_BUFS:
                    dve.wait_ge(sums_made, last_tile[products[n - PROD_BUFS]] // BATCH + 1)
                k = step[2] if step[0] == "block" else step[1]
                pair_made(dve, k)
                if step[0] == "block":
                    other = e_pair[:, k, :].unsqueeze(1).broadcast_to([P, 2, B])
                    nc.vector.tensor_tensor(to.rearrange("p (f b) -> p f b", f=2),
                                            ps[:].rearrange("p (f b) -> p f b", f=2), other,
                                            ALU.mult).then_inc(products_made, 1)
                else:
                    nc.vector.tensor_tensor(to[0:D, 0:B], ps[0:D, 0:B], e_pair[0:D, k, :],
                                            ALU.mult).then_inc(products_made, 1)

            waiting = None
            for i in range(len(order)):
                for s, f in one_hot_before.get(i, []):
                    one_hots(s, f)
                for n in split_before.get(i, []):
                    k_lo(n)
                if order[i][0] == "fields":
                    if order[i][1] in one_hot_no:
                        continue
                    waiting = order[i][1]
                    if waiting <= LO_AT_ONCE:
                        fields_lo(waiting)
                        waiting = None
                else:
                    if order[i][1] in one_hot_no and (order[i] == ("block", order[i][1], 0) or order[i][1] == 0):
                        one_hot_sum(order[i][1])
                    product(i)
                    if waiting is not None:
                        fields_lo(waiting)
                        waiting = None
            dve.wait_ge(weights_in, 3 * 16)
            for n in range(1, NC1, 2):
                dve.wait_ge(h1_summed, n + 1)
                nc.vector.tensor_scalar(h1_sb[:, n, :], h_ps(n), b1_sb[:, n:n + 1], 0.0, ALU.add,
                                        ALU.max).then_inc(h1_made[1], 1)
            dve.wait_ge(h2_summed, 2)
            nc.vector.tensor_scalar(h2_sb[:, 1, :], h_ps(NC1 + 1), b2_sb[:, 1:2], 0.0, ALU.add,
                                    ALU.max).then_inc(h2_made[1], 1)

        @block.tensor
        def _(pe):
            def one_hot_products(i, l):
                free_slot(pe, i)
                for f in (0, 1):
                    n = 2 * one_hot_no[l] + f
                    pe.wait_ge(table_lo_made, n + 1)
                    for c in range(SMALL_C):
                        m = SMALL_C * n + c
                        pe.wait_ge(one_hots_made, m + 1)
                        nc.tensor.matmul(slots[i % PSUM_BUFS][:, f * B:(f + 1) * B],
                                         table_parts[0:SMALL_P, n % TABLE_BUFS, c * 2 * D:(c + 1) * 2 * D],
                                         one_hot[0:SMALL_P, m % ONE_HOT_BUFS, :],
                                         start=(c == 0), stop=(c == SMALL_C - 1)).then_inc(one_hots_used, 1)

            def turn(i, l):
                g = gather_no[l]
                pe.wait_ge(gather_in[g % GATHER_BUFS], 2 * BT * 16 * (g // GATHER_BUFS + 1))
                free_slot(pe, i)
                for t in range(BT):
                    rows = gathered[:, g % GATHER_BUFS, t, :, :].rearrange("p f d -> p (f d)")
                    last = nc.tensor.transpose(slots[i % PSUM_BUFS][:, t * P:(t + 1) * P], rows, ident[:])
                last.then_inc(fields_turned, 1)

            def form(ps, weights, l, f):
                nc.tensor.matmul(ps, weights, e_moving[:, l % 2, f, 0, :], start=True, stop=False)
                return nc.tensor.matmul(ps, weights, e_moving[:, l % 2, f, 1, :], start=False, stop=True)

            def forms(i):
                step, ps = order[i], slots[i % PSUM_BUFS]
                l = step[1]
                free_slot(pe, i)
                pe.wait_ge(e_moved, 8 * (l + 1))
                if step[0] == "block":
                    b = blocks.index((l, step[2]))
                    n, at = 1 + b // BLOCKS_PER_CHUNK, b % BLOCKS_PER_CHUNK
                    split_landed(pe, n)
                    for f in (0, 1):
                        col = (2 * at + f) * 2 * D
                        last = form(ps[:, f * B:(f + 1) * B], split_place(n)[:, col:col + 2 * D], l, f)
                else:
                    split_landed(pe, 0)
                    last = form(ps[:, 0:B], k_diag[:, l * D:(l + 2) * D], l, 1)
                last.then_inc(forms_made, 1)

            def sums(b):
                pe.wait_ge(products_made, product_no[step_of_tile[BATCH * (b + 1) - 1]] + 1)
                kc, u = b // per_chunk, b % per_chunk
                if kc >= 2 and u == 0:
                    pe.wait_ge(z_copied, kc - 1)
                for t in range(BATCH * b, BATCH * (b + 1)):
                    i = step_of_tile[t]
                    h = t - (last_tile[i] + 1 - tiles_of(order[i]))
                    rows = P if order[i][0] == "block" else D
                    g = 32 * (t % BATCH)
                    last = nc.tensor.matmul(z_ps[kc % 2][g:g + 32, :], select[0:rows, u, :],
                                            prod[0:rows, product_no[i] % PROD_BUFS, h * B:(h + 1) * B],
                                            start=(u == 0), stop=(u == per_chunk - 1), skip_group_check=True)
                last.then_inc(sums_made, 1)

            def h1_sums(ns, kcs):
                pe.wait_ge(weights_in, 3 * 16)
                pe.wait_ge(z_copied, kcs[-1] + 1)
                for kc in kcs:
                    pe.wait_ge(dense_in[kc], 16 * sum(row // P == kc for _, row in spare_rows))
                for n in ns:
                    if kcs[0] == 0 and n % 2 == 0:
                        free_slot(pe, len(order) + n // 2)
                    for kc in kcs:
                        last = nc.tensor.matmul(h_ps(n), w1_sb[:, kc, n * P:(n + 1) * P], z_sb[:, kc, :],
                                                start=(kc == 0), stop=(kc == KC1 - 1), skip_group_check=True)
                    if kcs[-1] == KC1 - 1:
                        last.then_inc(h1_summed, 1)

            pe.wait_ge(consts_made, 1)
            pe.wait_ge(select_made, 4)
            for i in range(len(order) + LAG):
                if i == len(order):
                    h1_sums((0, 1), (0, 1, 2))
                if i < len(order):
                    if order[i][0] == "fields":
                        (one_hot_products if order[i][1] in one_hot_no else turn)(i, order[i][1])
                    else:
                        forms(i)
                for b in batches_after.get(i, []):
                    sums(b)

            h1_sums((2, 3), (0, 1, 2))
            h1_sums((0, 1, 2, 3), (3,))
            free_slot(pe, len(order) + NC1 // 2)
            for kc in range(KC2):
                pe.wait_ge(h1_made[kc % 2], kc // 2 + 1)
                for m in range(NC2):
                    last = nc.tensor.matmul(h_ps(NC1 + m), w2_sb[:, kc, m * P:(m + 1) * P], h1_sb[:, kc, :],
                                            start=(kc == 0), stop=(kc == KC2 - 1))
                    if kc == KC2 - 1:
                        last.then_inc(h2_summed, 1)
            for m in range(NC2):
                pe.wait_ge(h2_made[m], 1)
                last = nc.tensor.matmul(z_ps[0][0:1, :], w3_sb[:, m:m + 1], h2_sb[:, m, :],
                                        start=(m == 0), stop=(m == NC2 - 1))
            last.then_inc(y_summed, 1)


def kernel(**inputs):
    import numpy as np
    import concourse.bacc as bacc
    from concourse.bass_utils import run_bass_kernel_spmd

    arrays = {name: np.ascontiguousarray(a) for name, a in inputs.items()}
    laid = {f"tbl_{f}": arrays[f"tbl_{f}"] for f in range(FIELDS)}
    laid["ids"] = arrays["ids"]
    laid["small_ids"] = np.ascontiguousarray(arrays["ids"].T[list(SMALL_FIELDS)]).reshape(-1, 2 * B)
    laid["row_numbers"] = np.arange(SMALL_ROWS, dtype=np.float32).reshape(SMALL_P, SMALL_C)
    laid["dense_t"] = np.ascontiguousarray(arrays["dense_ctx"].T)
    k_all = arrays["L0_rec_kernel"]
    k = np.stack([k_all[:, n, :].T if turned else k_all[:, n, :] for n, turned in pair_order()], axis=1)

    def chunks(pairs, count):
        return np.ascontiguousarray(pairs.reshape(D, count, 2, -1).transpose(1, 2, 0, 3).reshape(count, P, -1))

    laid["k_diag_pairs"] = chunks(k[:, :DIAG_PAIRS], 1)[0]
    laid["k_pairs"] = chunks(k[:, DIAG_PAIRS:], CHUNKS - 1)
    laid["w1"] = np.ascontiguousarray(arrays["W_top1"][z_layout()[0]])
    laid["w2"] = arrays["W_top2"]
    vectors = [arrays[n].reshape(-1, P) for n in ("b_top1", "b_top2", "W_top3")]
    laid["b1_b2_w3"] = np.ascontiguousarray(np.concatenate(vectors).T)

    nc = bacc.Bacc("TRN2", target_bir_lowering=False, num_devices=1)
    ap = {n: nc.dram_tensor(n, a.shape, mybir.dt.from_np(a.dtype), kind="ExternalInput").ap() for n, a in laid.items()}
    out = nc.dram_tensor("y", (B, 1), F32, kind="ExternalOutput").ap()
    build(nc, ap["dense_t"], ap["ids"], ap["small_ids"], ap["row_numbers"], [ap[f"tbl_{f}"] for f in range(FIELDS)],
          ap["k_diag_pairs"], ap["k_pairs"], ap["w1"], ap["w2"], ap["b1_b2_w3"], out)
    r = run_bass_kernel_spmd(nc, [laid], core_ids=[0])
    return r.results[0]["y"]
```
